# Optimizing a Trainium2 kernel written in Bass

```python
import numpy as np
import jax
import jax.numpy as jnp

def _softmax(x, axis=-1):
    return jax.nn.softmax(x, axis=axis)

def _gelu(x):
    return jax.nn.gelu(x, approximate=True)

def _silu(x):
    return jax.nn.silu(x)

def _sigmoid(x):
    return jax.nn.sigmoid(x)

def _layernorm(x, axis=-1, eps=1e-05):
    m = jnp.mean(x, axis=axis, keepdims=True)
    v = jnp.var(x, axis=axis, keepdims=True)
    return (x - m) / jnp.sqrt(v + eps)

def _scatter_add(tgt, idx, src, axis=0):
    return tgt.at[idx].add(src)

def _segment_sum(src, seg, n):
    return jax.ops.segment_sum(src, seg, n)
kernel_name = 'mk_rec_standalone_d1_rec_r8_6376e6'

def setup_inputs(seed: int=0):
    np.random.seed(seed)
    _w = jnp.asarray

    def _rec_inputs():
        import jax
        import jax.numpy as jnp
        _rk = jax.random.key(seed)
        r_x = -0.00103678 + 1.00048 * jax.random.normal(jax.random.fold_in(_rk, 1), (512, 40, 16), jnp.float32)
        return r_x
    r_x = _rec_inputs()

    def _L0_rec_setup():
        import jax, jax.numpy as jnp
        import numpy as np
        B, M, D = (256, 40, 16)
        LAYERS = [128, 128, 128]
        key = jax.random.key(seed)
        ks = jax.random.split(key, 8)
        s = 0.05
        x = jax.random.normal(ks[0], (B, M, D), jnp.float32)
        w0 = jax.random.normal(ks[1], (128, M * M), jnp.float32) * s
        b0 = jax.random.normal(ks[2], (128,), jnp.float32) * s
        w1 = jax.random.normal(ks[3], (128, 64 * M), jnp.float32) * s
        b1 = jax.random.normal(ks[4], (128,), jnp.float32) * s
        w2 = jax.random.normal(ks[5], (128, 64 * M), jnp.float32) * s
        b2 = jax.random.normal(ks[6], (128,), jnp.float32) * s
        wl = jax.random.normal(ks[7], (1, 64 * 3), jnp.float32) * s
        return {'x': x, 'w0': w0, 'b0': b0, 'w1': w1, 'b1': b1, 'w2': w2, 'b2': b2, 'wl': wl}
    _L0_rec_all = _L0_rec_setup()
    _L0_rec_in = {k: v for k, v in _L0_rec_all.items() if k in ('w0', 'b0', 'w1', 'b1', 'w2', 'b2', 'wl')}
    del _L0_rec_all
    return {'r_x': r_x, 'L0_rec_w0': _L0_rec_in['w0'], 'L0_rec_b0': _L0_rec_in['b0'], 'L0_rec_w1': _L0_rec_in['w1'], 'L0_rec_b1': _L0_rec_in['b1'], 'L0_rec_w2': _L0_rec_in['w2'], 'L0_rec_b2': _L0_rec_in['b2'], 'L0_rec_wl': _L0_rec_in['wl']}

def reference(r_x, L0_rec_w0, L0_rec_b0, L0_rec_w1, L0_rec_b1, L0_rec_w2, L0_rec_b2, L0_rec_wl):
    import jax
    import jax.numpy as jnp

    def _L0_rec_ref(x, w0, b0, w1, b1, w2, b2, wl):
        import jax, jax.numpy as jnp
        import numpy as np
        B, M, D = (256, 40, 16)
        LAYERS = [128, 128, 128]
        _, m, _ = x.shape
        prev = x
        direct = []
        for w, b in ((w0, b0), (w1, b1), (w2, b2)):
            h = prev.shape[1]
            o = w.shape[0]
            wr = w.reshape(o, h, m)
            out = jnp.einsum('bhd,bmd,ohm->bod', prev, x, wr) + b[None, :, None]
            out = jax.nn.relu(out)
            half = o // 2
            prev = out[:, :half]
            direct.append(out[:, half:])
        feat = jnp.concatenate(direct, axis=1).sum(-1)
        return feat @ wl.T
    y = _L0_rec_ref(r_x, L0_rec_w0, L0_rec_b0, L0_rec_w1, L0_rec_b1, L0_rec_w2, L0_rec_b2, L0_rec_wl)
    return y

_drawn_inputs = setup_inputs


def setup_inputs(seed=0):
    import zlib

    import numpy as np

    out = dict(_drawn_inputs(seed))
    spreads = {}
    factors = {'L0_rec_b2': 8.0}
    for name, (base, spread) in spreads.items():
        noise = np.random.default_rng([zlib.crc32(name.encode()), seed]).standard_normal(out[name].shape)
        drawn = base * np.exp(spread * noise) if base else spread * noise
        out[name] = jnp.asarray(drawn.astype(out[name].dtype))
    for name, factor in factors.items():
        out[name] = (out[name] * factor).astype(out[name].dtype)
    return out
```

```python
import concourse.bass as bass
from concourse import mybir
from contextlib import ExitStack

B, M, D = 512, 40, 16
N = B * D
O = 128
H = O // 2
CHUNK = 1024
CHUNKS = N // CHUNK
BANK = 512
HALVES = CHUNK // BANK
CB = CHUNK // D

SHIFTS = M // 2 + 1
SPT = 3
T0 = SHIFTS // SPT
P0 = M * SPT
COPIES = 8
XROWS = M + SHIFTS - 1

T1 = M // 2
GT = 4
GROUPS = T1 // GT

ZT = 2
ZSLOTS = 4
I0 = (T0 + ZT - 1) // ZT
I1 = T1 // ZT
GI = GT // ZT
FIRST = I0 + I1
STEP = I0 + 2 * I1
MARK = 4


def cin_kernel(nc, x, x8, w0a, w0b, w1, w2, bias, wl, out):
    fp32 = mybir.dt.float32
    ALU = mybir.AluOpType
    RELU = mybir.ActivationFunctionType.Relu
    AX = mybir.AxisListType.X

    ctx = ExitStack()
    with ctx:
        def sb(name, shape):
            return ctx.enter_context(nc.sbuf_tensor(name, shape, fp32))

        def pb(name, shape):
            return ctx.enter_context(nc.psum_tensor(name, shape, fp32))

        def sem(name):
            return ctx.enter_context(nc.semaphore(name))

        w0a_sb = sb("w0a_sb", [P0, T0, O])
        w0b_sb = sb("w0b_sb", [P0, T0, O])
        w0_sb = sb("w0_sb", [P0, T0, O])
        w1_sb = sb("w1_sb", [128, T1, O])
        w2_sb = sb("w2_sb", [128, T1, H])
        bias_sb = sb("bias_sb", [128, 3])
        wl_sb = sb("wl_sb", [128, 2])
        own = sb("own", [P0, CHUNK])
        shifted = sb("shifted", [P0, T0, CHUNK])
        fields = sb("fields", [128, T1, CHUNK])
        z = sb("z", [128, ZSLOTS, ZT, CHUNK])
        direct01 = sb("direct01", [128, CHUNK])
        direct2 = sb("direct2", [128, BANK])
        feat01 = sb("feat01", [128, B])
        feat2 = sb("feat2", [H, B])
        y_sb = sb("y_sb", [1, B])

        acc0 = pb("acc0", [128, CHUNK])
        acc1 = pb("acc1", [128, CHUNK])
        acc2 = pb("acc2", [128, BANK])
        y_ps = pb("y_ps", [1, B])

        w0_here = sem("w0_here")
        w1_here = sem("w1_here")
        w2_here = sem("w2_here")
        small_here = sem("small_here")
        w0_summed = sem("w0_summed")
        own_here = sem("own_here")
        shifted_here = [sem(f"shifted_here{k}") for k in range(I0)]
        fields_here = [sem(f"fields_here{g}") for g in range(GROUPS)]
        z_made = sem("z_made")
        z_used = sem("z_used")
        acc2_read = sem("acc2_read")
        direct0_out = sem("direct0_out")
        direct1_out = sem("direct1_out")
        prev0_made = sem("prev0_made")
        prev1_made = sem("prev1_made")
        copy_made = sem("copy_made")
        feat01_done = sem("feat01_done")
        feat2_done = sem("feat2_done")
        y_done = sem("y_done")
        y_copied = sem("y_copied")
        y_stored = sem("y_stored")

        def tiles0(k):
            return ZT * k, min(ZT * (k + 1), T0)

        block = ctx.enter_context(nc.Block())

        @block.sync
        def _(sp):
            def load_own(c):
                src = bass.AP(x.tensor, x.offset + c * CHUNK, [[N, M], [0, SPT], [1, CHUNK]])
                sp.dma_start(own[:, :], src).then_inc(own_here, 16)

            def load_shifted(c, k):
                a, b = tiles0(k)
                for t in range(a, b):
                    src = bass.AP(x.tensor, x.offset + SPT * t * N + c * CHUNK, [[N, M], [N, SPT], [1, CHUNK]])
                    sp.dma_start(shifted[:, t, :], src).then_inc(shifted_here[k], 16)

            def load_fields(c, g):
                for j in range(GT * g, GT * (g + 1)):
                    src = bass.AP(x8.tensor, x8.offset + 2 * j * COPIES * N + c * CHUNK,
                                  [[N, 2 * COPIES], [0, H // COPIES], [1, CHUNK]])
                    sp.dma_start(fields[:, j, :], src).then_inc(fields_here[g], 16)

            load_own(0)
            load_shifted(0, 0)
            sp.dma_start(w0a_sb[:], w0a).then_inc(w0_here, 16)
            sp.dma_start(w0b_sb[:], w0b).then_inc(w0_here, 16)
            for k in range(1, I0):
                load_shifted(0, k)
            sp.dma_start(bias_sb[:], bias).then_inc(small_here, 16)
            sp.dma_start(wl_sb[:], wl).then_inc(small_here, 16)
            load_fields(0, 0)
            sp.dma_start(w1_sb[:], w1).then_inc(w1_here, 16)
            for g in range(1, GROUPS):
                load_fields(0, g)
            sp.dma_start(w2_sb[:], w2).then_inc(w2_here, 16)
            sp.wait_ge(z_made, I0)
            load_own(1)
            for k in range(I0):
                load_shifted(1, k)

            def turn(c, shifted_too):
                base = FIRST + STEP * c
                if shifted_too:
                    sp.wait_ge(z_made, base + I0)
                    load_own(c + 2)
                    for k in range(I0):
                        load_shifted(c + 2, k)
                for g in range(GROUPS):
                    sp.wait_ge(z_made, base + I0 + GI * (g + 1))
                    load_fields(c + 1, g)

            with sp.Fori(0, CHUNKS - 2) as c:
                turn(c, True)
            turn(CHUNKS - 2, False)
            sp.wait_ge(y_copied, 1)
            sp.dma_start(out, y_sb[0:1, :]).then_inc(y_stored, 16)
            sp.wait_ge(y_stored, 16)

        @block.vector
        def _(dve):

            def slot_free(n, slot_wait):
                if slot_wait:
                    dve.wait_ge(z_used, n - ZSLOTS + 1)

            def products0(c, n, slot, slot_wait=True):
                for k in range(I0):
                    a, b = tiles0(k)
                    if k == 0:
                        dve.wait_ge(own_here, 16 * (c + 1))
                    dve.wait_ge(shifted_here[k], 16 * (b - a) * (c + 1))
                    slot_free(n + k, slot_wait)
                    nc.vector.tensor_tensor(
                        z[0:P0, (slot + k) % ZSLOTS, 0:b - a, :], shifted[:, a:b, :],
                        own[:, None, :].to_broadcast([P0, b - a, CHUNK]), ALU.mult).then_inc(z_made, 1)

            def products12(n, slot, prev, k):
                slot_free(n + k, True)
                nc.vector.tensor_tensor(
                    z[:, (slot + k) % ZSLOTS, :, :],
                    prev[:, None, :].to_broadcast([128, ZT, CHUNK]),
                    fields[:, ZT * k:ZT * (k + 1), :], ALU.mult).then_inc(z_made, 1)

            def layer1(c, n, slot, sum2):
                dve.wait_ge(prev0_made, c + 1)
                for k in range(I1):
                    if k == MARK and sum2:
                        feature2(c - 1)
                    if k % GI == 0:
                        dve.wait_ge(fields_here[k // GI], 16 * GT * (c + 1))
                    products12(n, slot, acc0, k)

            def layer2(c, n, slot):
                dve.wait_ge(prev1_made, c + 1)
                for k in range(I1):
                    products12(n, slot, acc1, k)

            def feature01(c):
                dve.wait_ge(direct0_out, c + 1)
                dve.wait_ge(direct1_out, c + 1)
                nc.vector.tensor_reduce(feat01[:, bass.ds(c * CB, CB)],
                                        direct01[:, :].rearrange("p (b d) -> p b d", d=D),
                                        AX, ALU.add).then_inc(feat01_done, 1)

            def feature2(c):
                dve.wait_ge(acc2_read, c + 1)
                for i in range(HALVES):
                    nc.vector.tensor_reduce(feat2[:, bass.ds(c * CB + i * (CB // 2), CB // 2)],
                                            direct2[H * i:H * (i + 1), :].rearrange("p (b d) -> p b d", d=D),
                                            AX, ALU.add).then_inc(feat2_done, 1)

            dve.wait_ge(w0_here, 32)
            nc.vector.tensor_tensor(w0_sb[:], w0a_sb[:], w0b_sb[:], ALU.add).then_inc(w0_summed, 1)
            products0(0, 0, 0, slot_wait=False)
            layer1(0, I0, I0 % ZSLOTS, False)
            s = FIRST % ZSLOTS
            with dve.Fori(0, CHUNKS - 1) as c:
                n = FIRST + STEP * c
                products0(c + 1, n, s)
                feature01(c)
                layer2(c, n + I0, s + I0)
                layer1(c + 1, n + I0 + I1, s + I0 + I1, True)
            c = CHUNKS - 1
            feature01(c)
            layer2(c, FIRST + STEP * c, s)
            feature2(c)
            dve.wait_ge(y_done, 1)
            nc.vector.tensor_copy(y_sb[0:1, :], y_ps[0:1, :]).then_inc(y_copied, 1)

        @block.scalar
        def _(act):
            def evacuate(c, used, layer, acc, direct_out, prev_made):
                act.wait_ge(z_used, used)
                nc.scalar.activation(direct01[H * layer:H * (layer + 1), :], acc[H:O, :], RELU,
                                     bias=bias_sb[H:O, layer:layer + 1]).then_inc(direct_out, 1)
                act.wait_ge(direct_out, c + 1)
                nc.scalar.activation(acc[H:O, :], acc[0:H, :], RELU,
                                     bias=bias_sb[0:H, layer:layer + 1]).then_inc(copy_made, 1)
                act.wait_ge(copy_made, 2 * c + layer + 1)
                nc.scalar.activation(acc[0:H, :], acc[0:H, :], RELU,
                                     bias=bias_sb[0:H, layer:layer + 1]).then_inc(prev_made, 1)

            def evacuate2(c, used):
                act.wait_ge(z_used, used)
                nc.scalar.activation(direct2[:, :], acc2[:, :], RELU, bias=bias_sb[:, 2:3]).then_inc(acc2_read, 1)

            act.wait_ge(small_here, 32)
            evacuate(0, I0, 0, acc0, direct0_out, prev0_made)
            evacuate(0, FIRST, 1, acc1, direct1_out, prev1_made)

            with act.Fori(0, CHUNKS - 1) as c:
                n = FIRST + STEP * c
                act.wait_ge(feat01_done, c + 1)
                evacuate(c + 1, n + I0, 0, acc0, direct0_out, prev0_made)
                evacuate2(c, n + I0 + I1)
                evacuate(c + 1, n + STEP, 1, acc1, direct1_out, prev1_made)
            evacuate2(CHUNKS - 1, FIRST + STEP * (CHUNKS - 1) + I1)

        @block.tensor
        def _(pe):
            def layer0(n, slot):
                for k in range(I0):
                    a, b = tiles0(k)
                    pe.wait_ge(z_made, n + k + 1)
                    for t in range(a, b):
                        for h in range(HALVES):
                            last = nc.tensor.matmul(acc0[:, BANK * h:BANK * (h + 1)], w0_sb[:, t, :],
                                                    z[0:P0, (slot + k) % ZSLOTS, t - a, BANK * h:BANK * (h + 1)],
                                                    start=t == 0, stop=t == T0 - 1)
                    last.then_inc(z_used, 1)

            def layer1(n, slot):
                for k in range(I1):
                    pe.wait_ge(z_made, n + k + 1)
                    for t in range(ZT * k, ZT * (k + 1)):
                        for h in range(HALVES):
                            last = nc.tensor.matmul(acc1[:, BANK * h:BANK * (h + 1)], w1_sb[:, t, :],
                                                    z[:, (slot + k) % ZSLOTS, t % ZT, BANK * h:BANK * (h + 1)],
                                                    start=t == 0, stop=t == T1 - 1)
                    last.then_inc(z_used, 1)

            def layer2(n, slot):
                for k in range(I1):
                    pe.wait_ge(z_made, n + k + 1)
                    for t in range(ZT * k, ZT * (k + 1)):
                        for h in range(HALVES):
                            last = nc.tensor.matmul(acc2[H * h:H * (h + 1), :], w2_sb[:, t, :],
                                                    z[:, (slot + k) % ZSLOTS, t % ZT, BANK * h:BANK * (h + 1)],
                                                    start=t == 0, stop=t == T1 - 1)
                    last.then_inc(z_used, 1)

            pe.wait_ge(w0_summed, 1)
            layer0(0, 0)
            pe.wait_ge(w1_here, 16)
            layer1(I0, I0 % ZSLOTS)
            pe.wait_ge(w2_here, 16)

            s = FIRST % ZSLOTS
            with pe.Fori(0, CHUNKS - 1) as c:
                n = FIRST + STEP * c
                layer0(n, s)
                layer2(n + I0, s + I0)
                layer1(n + I0 + I1, s + I0 + I1)
            c = CHUNKS - 1
            layer2(FIRST + STEP * c, s)
            pe.wait_ge(feat01_done, CHUNKS)
            pe.wait_ge(feat2_done, HALVES * CHUNKS)
            nc.tensor.matmul(y_ps[0:1, :], wl_sb[:, 0:1], feat01[:, :], start=True, stop=False)
            nc.tensor.matmul(y_ps[0:1, :], wl_sb[0:H, 1:2], feat2[:, :], start=False, stop=True).then_inc(y_done, 1)


def kernel(r_x, L0_rec_w0, L0_rec_b0, L0_rec_w1, L0_rec_b1, L0_rec_w2, L0_rec_b2, L0_rec_wl):
    import numpy as np
    import concourse.bacc as bacc
    from concourse.bass_utils import run_bass_kernel_spmd

    fp32 = mybir.dt.float32
    xt = np.ascontiguousarray(np.asarray(r_x).transpose(1, 0, 2)).reshape(M, N)
    w0 = np.asarray(L0_rec_w0).reshape(O, M, M)
    m, t, i = np.meshgrid(np.arange(M), np.arange(T0), np.arange(SPT), indexing="ij")
    shift = SPT * t + i
    other = (m + shift) % M
    a = w0[:, m, other].transpose(1, 3, 2, 0)
    b = w0[:, other, m].transpose(1, 3, 2, 0)
    single = ((shift == 0) | (shift == M // 2)).transpose(0, 2, 1)
    b = np.where(single[..., None], np.zeros_like(b), b)

    def rows12(w):
        return np.asarray(w).reshape(O, H, T1, 2).transpose(3, 1, 2, 0).reshape(128, T1, O)

    b0, b1, b2 = (np.asarray(v) for v in (L0_rec_b0, L0_rec_b1, L0_rec_b2))
    wl = np.asarray(L0_rec_wl)[0]
    arrays = {
        "x": np.concatenate([xt, xt], 0)[:XROWS],
        "x8": np.repeat(xt, COPIES, 0),
        "w0a": a.reshape(P0, T0, O),
        "w0b": b.reshape(P0, T0, O),
        "w1": rows12(L0_rec_w1),
        "w2": rows12(L0_rec_w2)[:, :, H:],
        "bias": np.stack([b0, b1, np.concatenate([b2[H:], b2[H:]])], 1),
        "wl": np.stack([wl[:2 * H], np.concatenate([wl[2 * H:], wl[2 * H:]])], 1),
    }
    arrays = {k: np.ascontiguousarray(v) for k, v in arrays.items()}
    nc = bacc.Bacc("TRN2", target_bir_lowering=False, num_devices=1)
    args = [nc.dram_tensor(k, v.shape, fp32, kind="ExternalInput").ap() for k, v in arrays.items()]
    out = nc.dram_tensor("y", (B, 1), fp32, kind="ExternalOutput").ap()
    cin_kernel(nc, *args, out.rearrange("b one -> one b"))
    return run_bass_kernel_spmd(nc, [arrays], core_ids=[0]).results[0]["y"]
```

```python
import concourse.bass as bass
from concourse import mybir
from contextlib import ExitStack

B, M, D = 512, 40, 16
N = B * D
O = 128
H = O // 2
CHUNK = 512
CHUNKS = N // CHUNK
HALF = CHUNK // 2
CB = CHUNK // D

SPT = 3
T0 = (M // 2 + 1) // SPT
P0 = M * SPT
STARTS = M + SPT - 1

T1 = M // 2
G = 4
GROUPS = T1 // G
COPIES = 8

PAIR = 2
PAIRS = (T0 + PAIR - 1) // PAIR
RING = 2

LOOP_FROM, LOOP_TO = 2, CHUNKS - 2


def cin_kernel(nc, xs, xf, w0a, w0b, w1, w2, bias, wl, out):
    fp32 = mybir.dt.float32
    fp32r = mybir.dt.float32r
    ALU = mybir.AluOpType
    RELU = mybir.ActivationFunctionType.Relu
    AX = mybir.AxisListType.X

    ctx = ExitStack()
    with ctx:
        def sb(name, shape, dt=fp32):
            return ctx.enter_context(nc.sbuf_tensor(name, shape, dt))

        def pb(name, shape):
            return ctx.enter_context(nc.psum_tensor(name, shape, fp32))

        def sem(name):
            return ctx.enter_context(nc.semaphore(name))

        w0_sb = sb("w0_sb", [P0, T0, O])
        w1_hi = sb("w1_hi", [128, T1, O], fp32r)
        w1_lo = sb("w1_lo", [128, T1, O], fp32r)
        w2_sb = sb("w2_sb", [128, T1, H])
        bias_sb = sb("bias_sb", [128, 3])
        wl_sb = sb("wl_sb", [128, 3])
        own = sb("own", [P0, CHUNK])
        shifted = sb("shifted", [P0, T0 * CHUNK])
        fields = [sb(f"fields{p}", [128, T1 * CHUNK]) for p in range(2)]
        z0 = sb("z0", [P0, RING, PAIR * CHUNK])
        z1 = sb("z1", [128, RING, G * CHUNK])
        z1_hi = sb("z1_hi", [128, RING, G * CHUNK], fp32r)
        z1_lo = sb("z1_lo", [128, RING, G * CHUNK], fp32r)
        z2 = sb("z2", [128, RING, G * CHUNK])
        direct01 = sb("direct01", [128, CHUNK])
        direct2 = sb("direct2", [128, HALF])
        feat01 = sb("feat01", [128, B + CB])
        feat2 = sb("feat2", [H, B])
        y_sb = sb("y_sb", [1, B])
        raw = fields[1][:, 2 * G * CHUNK:]
        w1_raw = raw[:, 0:T1 * O]
        w0a_raw = raw[0:P0, T1 * O:(T1 + T0) * O]
        w0b_raw = raw[0:P0, (T1 + T0) * O:(T1 + 2 * T0) * O]
        RAW_GROUPS = range(2, GROUPS)

        own_ps = pb("own_ps", [P0, CHUNK])
        acc0 = pb("acc0", [128, CHUNK])
        prev0 = pb("prev0", [128, CHUNK])
        acc1 = pb("acc1", [128, CHUNK])
        prev1 = pb("prev1", [128, CHUNK])
        acc2 = pb("acc2", [128, HALF])
        y_ps = pb("y_ps", [1, B])

        w0_here = sem("w0_here")
        w1_here = sem("w1_here")
        w2_here = sem("w2_here")
        small_here = sem("small_here")
        w0_summed = sem("w0_summed")
        w1_hi_made = sem("w1_hi_made")
        w1_lo_made = sem("w1_lo_made")
        own_here = sem("own_here")
        own_in_psum = sem("own_in_psum")
        shifted_here = [sem(f"shifted_here{k}") for k in range(PAIRS)]
        fields_here = [[sem(f"fields{p}_here{g}") for g in range(GROUPS)] for p in range(2)]
        z0_made = sem("z0_made")
        z0_used = sem("z0_used")
        z1_made = sem("z1_made")
        z1_hi_made = sem("z1_hi_made")
        z1_lo_made = sem("z1_lo_made")
        z1_used = sem("z1_used")
        z2_made = sem("z2_made")
        z2_used = sem("z2_used")
        direct0_out = sem("direct0_out")
        direct1_out = sem("direct1_out")
        direct2_out = sem("direct2_out")
        prev0_made = sem("prev0_made")
        prev1_made = sem("prev1_made")
        feat_cleared = sem("feat_cleared")
        feat01_done = sem("feat01_done")
        feat2_done = sem("feat2_done")
        y_done = sem("y_done")
        y_copied = sem("y_copied")
        y_stored = sem("y_stored")

        def pair(k):
            return PAIR * k, min(PAIR * (k + 1), T0)

        def turns(eng, turn, loop_to=LOOP_TO):
            for c in range(-2, LOOP_FROM):
                turn(c, c % 2)
            with eng.Fori(LOOP_FROM, loop_to, 2) as c:
                turn(c, 0)
                turn(c + 1, 1)
            for c in range(loop_to, CHUNKS):
                turn(c, c % 2)

        def parts(c):
            if isinstance(c, int):
                return c + 2 < CHUNKS, 0 <= c + 1 < CHUNKS, c >= 0
            return True, True, True

        block = ctx.enter_context(nc.Block())

        @block.sync
        def _(sp):
            def load_own(q):
                src = bass.AP(xs.tensor, xs.offset + q * (STARTS * T0 * CHUNK),
                              [[T0 * CHUNK, M], [0, SPT], [1, CHUNK]])
                sp.dma_start(own[:, :], src).then_inc(own_here, 16)

            def load_shifted(q, k):
                a, b = pair(k)
                src = bass.AP(xs.tensor, xs.offset + q * (STARTS * T0 * CHUNK) + a * CHUNK,
                              [[T0 * CHUNK, M], [T0 * CHUNK, SPT], [1, (b - a) * CHUNK]])
                sp.dma_start(shifted[:, a * CHUNK:b * CHUNK], src).then_inc(shifted_here[k], 16)

            def load_fields(q, parity, g):
                src = bass.AP(xf.tensor, xf.offset + (q * GROUPS + g) * (2 * COPIES * G * CHUNK),
                              [[G * CHUNK, 2 * COPIES], [0, H // COPIES], [1, G * CHUNK]])
                sp.dma_start(fields[parity][:, g * G * CHUNK:(g + 1) * G * CHUNK],
                             src).then_inc(fields_here[parity][g], 16)

            load_own(0)
            load_shifted(0, 0)
            sp.dma_start(w0a_raw, w0a).then_inc(w0_here, 16)
            sp.dma_start(w0b_raw, w0b).then_inc(w0_here, 16)
            for k in range(1, PAIRS):
                load_shifted(0, k)
            sp.dma_start(bias_sb[:], bias).then_inc(small_here, 16)
            sp.dma_start(wl_sb[:], wl).then_inc(small_here, 16)
            load_fields(0, 0, 0)
            sp.dma_start(w1_raw, w1).then_inc(w1_here, 16)

            def turn(c, parity):
                if not isinstance(c, int) or c + 3 < CHUNKS:
                    sp.wait_ge(own_in_psum, c + 3)
                    load_own(c + 3)
                    for k in range(PAIRS):
                        sp.wait_ge(z0_made, PAIRS * (c + 2) + k + 1)
                        load_shifted(c + 3, k)
                if isinstance(c, int) and c == -2:
                    for g in range(1, GROUPS):
                        load_fields(0, 0, g)
                    sp.dma_start(w2_sb[:], w2).then_inc(w2_here, 16)
                elif isinstance(c, int) and c == -1:
                    for g in range(GROUPS):
                        if g == RAW_GROUPS[0]:
                            sp.wait_ge(w0_summed, 1)
                            sp.wait_ge(w1_lo_made, 1)
                        load_fields(1, 1, g)
                elif not isinstance(c, int) or c + 2 < CHUNKS:
                    for g in range(GROUPS):
                        sp.wait_ge(z2_made, GROUPS * c + g + 1)
                        load_fields(c + 2, parity, g)

            turns(sp, turn, loop_to=LOOP_TO - 2)
            sp.wait_ge(y_copied, 1)
            sp.dma_start(out, y_sb[0:1, :]).then_inc(y_stored, 16)
            sp.wait_ge(y_stored, 16)

        @block.vector
        def _(dve):
            def product0(q, k):
                a, b = pair(k)
                if k == 0:
                    dve.wait_ge(own_in_psum, q + 1)
                dve.wait_ge(shifted_here[k], 16 * (q + 1))
                if not isinstance(q, int) or PAIRS * q + k >= RING:
                    dve.wait_ge(z0_used, PAIRS * q + k - RING + 1)
                nc.vector.tensor_tensor(
                    z0[:, k % RING, 0:(b - a) * CHUNK].rearrange("p (t n) -> p t n", n=CHUNK),
                    own_ps[:, None, :].to_broadcast([P0, b - a, CHUNK]),
                    shifted[:, a * CHUNK:b * CHUNK].rearrange("p (t n) -> p t n", n=CHUNK),
                    ALU.mult).then_inc(z0_made, 1)

            def product(z, slot, prev, parity, g):
                return nc.vector.tensor_tensor(
                    z[:, slot, :].rearrange("p (t n) -> p t n", n=CHUNK),
                    prev[:, None, :].to_broadcast([128, G, CHUNK]),
                    fields[parity][:, g * G * CHUNK:(g + 1) * G * CHUNK].rearrange("p (t n) -> p t n", n=CHUNK),
                    ALU.mult)

            def product1(q, parity, g):
                if g == 0:
                    dve.wait_ge(prev0_made, q + 1)
                dve.wait_ge(fields_here[parity][g], 8 * (q - parity) + 16)
                if not isinstance(q, int) or GROUPS * q + g >= RING:
                    dve.wait_ge(z1_lo_made, GROUPS * q + g - RING + 1)
                product(z1, (GROUPS * parity + g) % RING, prev0, parity, g).then_inc(z1_made, 1)

            def product2(q, parity, g):
                if g == 0:
                    dve.wait_ge(prev1_made, q + 1)
                if not isinstance(q, int) or GROUPS * q + g >= RING:
                    dve.wait_ge(z2_used, GROUPS * q + g - RING + 1)
                product(z2, (GROUPS * parity + g) % RING, prev1, parity, g).then_inc(z2_made, 1)

            def sum01(c, rows=slice(0, 128)):
                if rows.start == 0:
                    dve.wait_ge(direct0_out, c + 2)
                if rows.stop == 128:
                    dve.wait_ge(direct1_out, c + 1)
                nc.vector.tensor_reduce(feat01[rows, bass.ds((c + 1) * CB, CB)],
                                        direct01[rows, :].rearrange("p (b d) -> p b d", d=D),
                                        AX, ALU.add).then_inc(feat01_done, 1)

            def sum2(q):
                dve.wait_ge(direct2_out, q + 1)
                for i in range(2):
                    nc.vector.tensor_reduce(feat2[:, bass.ds(q * CB + i * (CB // 2), CB // 2)],
                                            direct2[H * i:H * (i + 1), :].rearrange("p (b d) -> p b d", d=D),
                                            AX, ALU.add).then_inc(feat2_done, 1)

            def turn(c, parity):
                layer0, layer1, layer2 = parts(c)

                def p0(k):
                    if layer0:
                        product0(c + 2, k)

                def p1(g):
                    if layer1:
                        product1(c + 1, 1 - parity, g)

                def p2(g):
                    if layer2:
                        product2(c, parity, g)

                p1(0)
                p0(0)
                p0(1)
                p1(1)
                p0(2)
                p0(3)
                p2(0)
                p1(2)
                if not isinstance(c, int) or 0 <= c < CHUNKS - 1:
                    sum01(c)
                elif c == -1:
                    sum01(c, slice(0, H))
                elif c == CHUNKS - 1:
                    sum01(c, slice(H, 128))
                p2(1)
                p1(3)
                if not isinstance(c, int) or c >= 1:
                    sum2(c - 1)
                p2(2)
                p1(4)
                p2(3)
                p2(4)

            dve.wait_ge(w0_here, 32)
            nc.vector.tensor_tensor(w0_sb[:], w0a_raw.rearrange("p (t o) -> p t o", o=O),
                                    w0b_raw.rearrange("p (t o) -> p t o", o=O), ALU.add).then_inc(w0_summed, 1)
            nc.vector.memset(feat01[H:128, 0:CB], 0.0).then_inc(feat_cleared, 1)
            nc.vector.memset(feat01[0:H, B:B + CB], 0.0).then_inc(feat_cleared, 1)
            turns(dve, turn)
            sum2(CHUNKS - 1)
            dve.wait_ge(y_done, 1)
            nc.vector.tensor_copy(y_sb[0:1, :], y_ps[0:1, :]).then_inc(y_copied, 1)

        @block.gpsimd
        def _(pool):
            pool.wait_ge(w1_hi_made, 1)
            nc.gpsimd.tensor_tensor(w1_lo[:].rearrange("p t o -> p (t o)"), w1_raw,
                                    w1_hi[:].rearrange("p t o -> p (t o)").bitcast(fp32),
                                    ALU.subtract).then_inc(w1_lo_made, 1)

            def turn(c, parity):
                if not parts(c)[1]:
                    return
                for g in range(GROUPS):
                    n = GROUPS * (c + 1) + g
                    slot = (GROUPS * (1 - parity) + g) % RING
                    pool.wait_ge(z1_hi_made, n + 1)
                    if not isinstance(c, int) or n >= RING:
                        pool.wait_ge(z1_used, n - RING + 1)
                    nc.gpsimd.tensor_tensor(z1_lo[:, slot, :], z1[:, slot, :], z1_hi[:, slot, :].bitcast(fp32),
                                            ALU.subtract).then_inc(z1_lo_made, 1)

            turns(pool, turn)

        @block.scalar
        def _(act):
            def split(q, parity, g):
                n = GROUPS * q + g
                slot = (GROUPS * parity + g) % RING
                act.wait_ge(z1_made, n + 1)
                if not isinstance(q, int) or n >= RING:
                    act.wait_ge(z1_used, n - RING + 1)
                nc.scalar.copy(z1_hi[:, slot, :], z1[:, slot, :]).then_inc(z1_hi_made, 1)

            def own_to_psum(q):
                act.wait_ge(own_here, 16 * (q + 1))
                if not isinstance(q, int) or q >= 1:
                    act.wait_ge(z0_made, PAIRS * q)
                nc.scalar.copy(own_ps[:, :], own[:, :]).then_inc(own_in_psum, 1)

            def evacuate(layer, acc, prev, direct_out, prev_made):
                nc.scalar.activation(direct01[H * layer:H * (layer + 1), :], acc[H:O, :], RELU,
                                     bias=bias_sb[H:O, layer:layer + 1]).then_inc(direct_out, 1)
                nc.scalar.activation(prev[0:H, :], acc[0:H, :], RELU, bias=bias_sb[0:H, layer:layer + 1])
                nc.scalar.activation(prev[H:O, :], acc[0:H, :], RELU,
                                     bias=bias_sb[0:H, layer:layer + 1]).then_inc(prev_made, 1)

            def evacuate0(q):
                act.wait_ge(z0_used, PAIRS * (q + 1))
                if not isinstance(q, int) or q >= 1:
                    act.wait_ge(feat01_done, q)
                    act.wait_ge(z1_made, GROUPS * q)
                evacuate(0, acc0, prev0, direct0_out, prev0_made)

            def evacuate1(q):
                act.wait_ge(z1_used, GROUPS * (q + 1))
                if not isinstance(q, int) or q >= 1:
                    act.wait_ge(z2_made, GROUPS * q)
                    act.wait_ge(feat01_done, q + 1)
                evacuate(1, acc1, prev1, direct1_out, prev1_made)

            def evacuate2(q):
                act.wait_ge(z2_used, GROUPS * (q + 1))
                if not isinstance(q, int) or q >= 1:
                    act.wait_ge(feat2_done, 2 * q)
                nc.scalar.activation(direct2[:, :], acc2[:, :], RELU, bias=bias_sb[:, 2:3]).then_inc(direct2_out, 1)

            def turn(c, parity):
                layer0, layer1, layer2 = parts(c)
                if layer0:
                    own_to_psum(c + 2)
                if isinstance(c, int) and c == -2:
                    act.wait_ge(w1_here, 16)
                    nc.scalar.copy(w1_hi[:].rearrange("p t o -> p (t o)"), w1_raw).then_inc(w1_hi_made, 1)
                    act.wait_ge(small_here, 32)
                if layer1:
                    split(c + 1, 1 - parity, 0)
                if layer2:
                    evacuate1(c)
                if not isinstance(c, int) or c >= 1:
                    evacuate2(c - 1)
                if layer1:
                    for g in range(1, GROUPS):
                        split(c + 1, 1 - parity, g)
                if layer0:
                    evacuate0(c + 2)

            turns(act, turn)
            evacuate2(CHUNKS - 1)

        @block.tensor
        def _(pe):
            def sums0(q, k):
                a, b = pair(k)
                if k == 0 and (not isinstance(q, int) or q >= 1):
                    pe.wait_ge(prev0_made, q)
                pe.wait_ge(z0_made, PAIRS * q + k + 1)
                for t in range(a, b):
                    last = nc.tensor.matmul(acc0[:, :], w0_sb[:, t, :],
                                            z0[:, k % RING, (t - a) * CHUNK:(t - a + 1) * CHUNK],
                                            start=t == 0, stop=t == T0 - 1)
                last.then_inc(z0_used, 1)

            def sums1(q, parity, g):
                slot = (GROUPS * parity + g) % RING
                if g == 0 and (not isinstance(q, int) or q >= 1):
                    pe.wait_ge(prev1_made, q)
                pe.wait_ge(z1_lo_made, GROUPS * q + g + 1)
                for t in range(G):
                    at = slice(t * CHUNK, (t + 1) * CHUNK)
                    j = G * g + t
                    nc.tensor.matmul(acc1[:, :], w1_hi[:, j, :], z1_hi[:, slot, at], start=j == 0, stop=False)
                    nc.tensor.matmul(acc1[:, :], w1_hi[:, j, :], z1_lo[:, slot, at], start=False, stop=False)
                    last = nc.tensor.matmul(acc1[:, :], w1_lo[:, j, :], z1_hi[:, slot, at],
                                            start=False, stop=j == T1 - 1)
                last.then_inc(z1_used, 1)

            def sums2(q, parity, g):
                slot = (GROUPS * parity + g) % RING
                if g == 0 and (not isinstance(q, int) or q >= 1):
                    pe.wait_ge(direct2_out, q)
                pe.wait_ge(z2_made, GROUPS * q + g + 1)
                for t in range(G):
                    j = G * g + t
                    for h in range(2):
                        at = t * CHUNK + h * HALF
                        last = nc.tensor.matmul(acc2[H * h:H * (h + 1), :], w2_sb[:, j, :],
                                                z2[:, slot, at:at + HALF], start=j == 0, stop=j == T1 - 1)
                last.then_inc(z2_used, 1)

            def turn(c, parity):
                layer0, layer1, layer2 = parts(c)
                if isinstance(c, int) and c == -1:
                    pe.wait_ge(w1_hi_made, 1)
                    pe.wait_ge(w1_lo_made, 1)
                if isinstance(c, int) and c == 0:
                    pe.wait_ge(w2_here, 16)

                def s0(k):
                    if layer0:
                        sums0(c + 2, k)

                def s1(g):
                    if layer1:
                        sums1(c + 1, 1 - parity, g)

                def s2(g):
                    if layer2:
                        sums2(c, parity, g)

                s0(0)
                s0(1)
                s1(0)
                s0(2)
                s0(3)
                s1(1)
                s2(0)
                s2(1)
                s1(2)
                s2(2)
                s1(3)
                s2(3)
                s1(4)
                s2(4)

            pe.wait_ge(w0_summed, 1)
            turns(pe, turn)
            pe.wait_ge(small_here, 32)
            pe.wait_ge(feat_cleared, 2)
            pe.wait_ge(feat01_done, CHUNKS + 1)
            pe.wait_ge(feat2_done, 2 * CHUNKS)
            nc.tensor.matmul(y_ps[0:1, :], wl_sb[:, 0:1], feat01[:, 0:B], start=True, stop=False)
            nc.tensor.matmul(y_ps[0:1, :], wl_sb[:, 1:2], feat01[:, CB:B + CB], start=False, stop=False)
            nc.tensor.matmul(y_ps[0:1, :], wl_sb[0:H, 2:3], feat2[:, :], start=False, stop=True).then_inc(y_done, 1)


def kernel(r_x, L0_rec_w0, L0_rec_b0, L0_rec_w1, L0_rec_b1, L0_rec_w2, L0_rec_b2, L0_rec_wl):
    import numpy as np
    import concourse.bacc as bacc
    from concourse.bass_utils import run_bass_kernel_spmd

    fp32 = mybir.dt.float32
    xt = np.asarray(r_x).transpose(1, 0, 2).reshape(M, CHUNKS, CHUNK)
    start, tile = np.arange(STARTS)[:, None], np.arange(T0)[None, :]
    xs = xt[(start + SPT * tile) % M].transpose(2, 0, 1, 3)
    xf = xt.reshape(GROUPS, G, 2, CHUNKS, CHUNK).transpose(3, 0, 2, 1, 4)
    xf = np.repeat(xf[:, :, :, None], COPIES, 3)

    w0 = np.asarray(L0_rec_w0).reshape(O, M, M)
    m, i, t = np.meshgrid(np.arange(M), np.arange(SPT), np.arange(T0), indexing="ij")
    shift = SPT * t + i
    other = (m + shift) % M
    a = w0[:, m, other].transpose(1, 2, 3, 0)
    b = w0[:, other, m].transpose(1, 2, 3, 0)
    b = np.where(((shift == 0) | (shift == M // 2))[..., None], np.zeros_like(b), b)

    def rows12(w):
        return np.asarray(w).reshape(O, H, T1, 2).transpose(3, 1, 2, 0).reshape(128, T1, O)

    b0, b1, b2 = (np.asarray(v) for v in (L0_rec_b0, L0_rec_b1, L0_rec_b2))
    l0, l1, l2 = np.asarray(L0_rec_wl)[0].reshape(3, H)
    none = np.zeros_like(l0)
    arrays = {
        "xs": xs,
        "xf": xf,
        "w0a": a.reshape(P0, T0 * O),
        "w0b": b.reshape(P0, T0 * O),
        "w1": rows12(L0_rec_w1).reshape(128, T1 * O),
        "w2": rows12(L0_rec_w2)[:, :, H:],
        "bias": np.stack([b0, b1, np.concatenate([b2[H:], b2[H:]])], 1),
        "wl": np.stack([np.concatenate(v) for v in ([l0, none], [none, l1], [l2, none])], 1),
    }
    arrays = {k: np.ascontiguousarray(v) for k, v in arrays.items()}
    nc = bacc.Bacc("TRN2", target_bir_lowering=False, num_devices=1)
    args = [nc.dram_tensor(k, v.shape, fp32, kind="ExternalInput").ap() for k, v in arrays.items()]
    out = nc.dram_tensor("y", (B, 1), fp32, kind="ExternalOutput").ap()
    cin_kernel(nc, *args, out.rearrange("b one -> one b"))
    return run_bass_kernel_spmd(nc, [arrays], core_ids=[0]).results[0]["y"]
```

```python
import concourse.bass as bass
from concourse import mybir
from contextlib import ExitStack

B, M, D = 512, 40, 16
N = B * D
O = 128
H = O // 2
CHUNK = 512
CHUNKS = N // CHUNK
HALF = CHUNK // 2
CB = CHUNK // D

SPT = 3
T0 = (M // 2 + 1) // SPT
P0 = M * SPT
STARTS = M + SPT - 1

T1 = M // 2
G = 4
GROUPS = T1 // G
COPIES = 8

PAIR = 2
PAIRS = (T0 + PAIR - 1) // PAIR
RING = 2
SPLIT = 2
SPLITS = T1 // SPLIT
SPLIT_RING = 4

WHOLE = 4
WARM_UPS = 5

LOOP_FROM, LOOP_TO = 2, CHUNKS - 2


def cin_kernel(nc, xs, xf, w0a, w0b, w1, w2, bias, wl, out):
    fp32 = mybir.dt.float32
    fp32r = mybir.dt.float32r
    ALU = mybir.AluOpType
    RELU = mybir.ActivationFunctionType.Relu
    AX = mybir.AxisListType.X

    ctx = ExitStack()
    with ctx:
        def sb(name, shape, dt=fp32):
            return ctx.enter_context(nc.sbuf_tensor(name, shape, dt))

        def pb(name, shape):
            return ctx.enter_context(nc.psum_tensor(name, shape, fp32))

        def sem(name):
            return ctx.enter_context(nc.semaphore(name))

        w0_sb = sb("w0_sb", [P0, T0, O])
        w1_hi = sb("w1_hi", [128, T1, O], fp32r)
        w1_lo = sb("w1_lo", [128, T1, O], fp32r)
        w2_sb = sb("w2_sb", [128, T1, H])
        bias_sb = sb("bias_sb", [128, 3])
        wl_sb = sb("wl_sb", [128, 3])
        own = sb("own", [P0, CHUNK])
        shifted = sb("shifted", [P0, T0 * CHUNK])
        fields = [sb(f"fields{p}", [128, T1 * CHUNK]) for p in range(2)]
        z0 = sb("z0", [P0, RING, PAIR * CHUNK])
        z1 = sb("z1", [128, SPLIT_RING, SPLIT * CHUNK])
        z1_hi = sb("z1_hi", [128, SPLIT_RING, SPLIT * CHUNK], fp32r)
        z1_lo = sb("z1_lo", [128, SPLIT_RING, SPLIT * CHUNK], fp32r)
        z2 = sb("z2", [128, RING, G * CHUNK])
        direct01 = sb("direct01", [128, CHUNK])
        direct2 = sb("direct2", [128, HALF])
        feat01 = sb("feat01", [128, B + CB])
        feat2 = sb("feat2", [H, B])
        y_sb = direct01[0:1, 0:B]
        raw = fields[1][:, 2 * G * CHUNK:]
        w1_raw = raw[:, 0:T1 * O]
        w0a_raw = raw[0:P0, T1 * O:(T1 + T0) * O]
        w0b_raw = raw[0:P0, (T1 + T0) * O:(T1 + 2 * T0) * O]

        own_ps = pb("own_ps", [P0, CHUNK])
        acc0 = pb("acc0", [128, CHUNK])
        prev0 = pb("prev0", [128, CHUNK])
        acc1 = pb("acc1", [128, CHUNK])
        prev1 = pb("prev1", [128, CHUNK])
        acc2 = pb("acc2", [128, HALF])
        y_ps = pb("y_ps", [1, B])

        w0_here = sem("w0_here")
        w1_here = sem("w1_here")
        w2_here = sem("w2_here")
        small_here = sem("small_here")
        w0_summed = sem("w0_summed")
        w1_hi_made = sem("w1_hi_made")
        w1_lo_made = sem("w1_lo_made")
        own_here = sem("own_here")
        own_in_psum = sem("own_in_psum")
        shifted_here = [sem(f"shifted_here{k}") for k in range(PAIRS)]
        fields_here = [[sem(f"fields{p}_here{g}") for g in range(GROUPS)] for p in range(2)]
        z0_made = sem("z0_made")
        z0_used = sem("z0_used")
        z1_made = sem("z1_made")
        z1_hi_made = sem("z1_hi_made")
        z1_lo_made = sem("z1_lo_made")
        z1_used = sem("z1_used")
        z2_made = sem("z2_made")
        z2_used = sem("z2_used")
        direct0_out = sem("direct0_out")
        direct1_out = sem("direct1_out")
        direct2_out = sem("direct2_out")
        prev0_made = sem("prev0_made")
        prev1_made = sem("prev1_made")
        zeros_made = sem("zeros_made")
        feat_cleared = sem("feat_cleared")
        feat01_done = sem("feat01_done")
        feat2_done = sem("feat2_done")
        y_done = sem("y_done")
        y_copied = sem("y_copied")
        y_stored = sem("y_stored")

        def pair(k):
            return PAIR * k, min(PAIR * (k + 1), T0)

        def split(q, parity, s):
            return SPLITS * q + s, (SPLITS * parity + s) % SPLIT_RING

        def whole(q, s):
            return isinstance(q, int) and q == 0 and s < WHOLE

        def splits(n):
            return n + 1 - WHOLE

        def turns(eng, turn, turn_from=-2, loop_to=LOOP_TO):
            for c in range(turn_from, LOOP_FROM):
                turn(c, c % 2)
            with eng.Fori(LOOP_FROM, loop_to, 2) as c:
                turn(c, 0)
                turn(c + 1, 1)
            for c in range(loop_to, CHUNKS):
                turn(c, c % 2)

        def parts(c):
            if isinstance(c, int):
                return c + 2 < CHUNKS, 0 <= c + 1 < CHUNKS, c >= 0
            return True, True, True

        block = ctx.enter_context(nc.Block())

        @block.sync
        def _(sp):
            def load_own(q):
                src = bass.AP(xs.tensor, xs.offset + q * (STARTS * T0 * CHUNK),
                              [[T0 * CHUNK, M], [0, SPT], [1, CHUNK]])
                sp.dma_start(own[:, :], src).then_inc(own_here, 16)

            def load_shifted(q, k):
                a, b = pair(k)
                src = bass.AP(xs.tensor, xs.offset + q * (STARTS * T0 * CHUNK) + a * CHUNK,
                              [[T0 * CHUNK, M], [T0 * CHUNK, SPT], [1, (b - a) * CHUNK]])
                sp.dma_start(shifted[:, a * CHUNK:b * CHUNK], src).then_inc(shifted_here[k], 16)

            def load_fields(q, parity, g):
                src = bass.AP(xf.tensor, xf.offset + (q * GROUPS + g) * (2 * COPIES * G * CHUNK),
                              [[G * CHUNK, 2 * COPIES], [0, H // COPIES], [1, G * CHUNK]])
                sp.dma_start(fields[parity][:, g * G * CHUNK:(g + 1) * G * CHUNK],
                             src).then_inc(fields_here[parity][g], 16)

            def reload_own(q):
                sp.wait_ge(own_in_psum, q)
                load_own(q)

            def reload_shifted(q, k):
                sp.wait_ge(z0_made, PAIRS * (q - 1) + k + 1)
                load_shifted(q, k)

            load_own(0)
            load_shifted(0, 0)
            sp.dma_start(w0a_raw, w0a).then_inc(w0_here, 16)
            sp.dma_start(w0b_raw, w0b).then_inc(w0_here, 16)
            for k in range(1, PAIRS):
                load_shifted(0, k)
            sp.dma_start(bias_sb[:], bias).then_inc(small_here, 16)
            sp.dma_start(wl_sb[:], wl).then_inc(small_here, 16)
            load_fields(0, 0, 0)
            sp.dma_start(w1_raw, w1).then_inc(w1_here, 16)

            def turn(c, parity):
                if isinstance(c, int) and c == -2:
                    load_fields(0, 0, 1)
                    reload_own(1)
                    reload_shifted(1, 0)
                    load_fields(0, 0, 2)
                    reload_shifted(1, 1)
                    load_fields(0, 0, 3)
                    reload_shifted(1, 2)
                    load_fields(0, 0, 4)
                    reload_shifted(1, 3)
                    return
                if isinstance(c, int) and c == -1:
                    reload_own(2)
                    reload_shifted(2, 0)
                    sp.dma_start(w2_sb[:], w2).then_inc(w2_here, 16)
                    load_fields(1, 1, 0)
                    load_fields(1, 1, 1)
                    reload_shifted(2, 1)
                    sp.wait_ge(w0_summed, 1)
                    sp.wait_ge(w1_lo_made, 1)
                    sp.wait_ge(z1_used, WHOLE)
                    load_fields(1, 1, 2)
                    reload_shifted(2, 2)
                    load_fields(1, 1, 3)
                    load_fields(1, 1, 4)
                    reload_shifted(2, 3)
                    return
                if not isinstance(c, int) or c + 3 < CHUNKS:
                    reload_own(c + 3)
                    for k in range(PAIRS):
                        reload_shifted(c + 3, k)
                if not isinstance(c, int) or c + 2 < CHUNKS:
                    for g in range(GROUPS):
                        sp.wait_ge(z2_made, GROUPS * c + g + 1)
                        load_fields(c + 2, parity, g)

            turns(sp, turn, loop_to=LOOP_TO - 2)
            sp.wait_ge(y_copied, 1)
            sp.dma_start(out, y_sb).then_inc(y_stored, 16)
            sp.wait_ge(y_stored, 16)

        @block.vector
        def _(dve):
            def product0(q, k):
                a, b = pair(k)
                if k == 0:
                    dve.wait_ge(own_in_psum, q + 1)
                dve.wait_ge(shifted_here[k], 16 * (q + 1))
                if not isinstance(q, int) or PAIRS * q + k >= RING:
                    dve.wait_ge(z0_used, PAIRS * q + k - RING + 1)
                nc.vector.tensor_tensor(
                    z0[:, k % RING, 0:(b - a) * CHUNK].rearrange("p (t n) -> p t n", n=CHUNK),
                    own_ps[:, None, :].to_broadcast([P0, b - a, CHUNK]),
                    shifted[:, a * CHUNK:b * CHUNK].rearrange("p (t n) -> p t n", n=CHUNK),
                    ALU.mult).then_inc(z0_made, 1)

            def product(z, prev, parity, a, b):
                return nc.vector.tensor_tensor(
                    z.rearrange("p (t n) -> p t n", n=CHUNK),
                    prev[:, None, :].to_broadcast([128, b - a, CHUNK]),
                    fields[parity][:, a * CHUNK:b * CHUNK].rearrange("p (t n) -> p t n", n=CHUNK), ALU.mult)

            def product1(q, parity, s):
                n, slot = split(q, parity, s)
                if s == 0:
                    dve.wait_ge(prev0_made, q + 1)
                if SPLIT * s % G == 0:
                    dve.wait_ge(fields_here[parity][SPLIT * s // G], 8 * (q - parity) + 16)
                if isinstance(q, int) and SPLIT_RING <= n < SPLIT_RING + WHOLE:
                    dve.wait_ge(z1_used, n - SPLIT_RING + 1)
                elif not isinstance(q, int) or n >= SPLIT_RING:
                    dve.wait_ge(z1_lo_made, splits(n - SPLIT_RING))
                product(z1[:, slot, :], prev0, parity, SPLIT * s, SPLIT * (s + 1)).then_inc(z1_made, 1)

            def product2(q, parity, g):
                if g == 0:
                    dve.wait_ge(prev1_made, q + 1)
                if not isinstance(q, int) or GROUPS * q + g >= RING:
                    dve.wait_ge(z2_used, GROUPS * q + g - RING + 1)
                product(z2[:, (GROUPS * parity + g) % RING, :], prev1, parity, G * g, G * (g + 1)).then_inc(z2_made, 1)

            def sum01(c, rows=slice(0, 128)):
                if rows.start == 0:
                    dve.wait_ge(direct0_out, c + 2)
                if rows.stop == 128:
                    dve.wait_ge(direct1_out, c + 1)
                nc.vector.tensor_reduce(feat01[rows, bass.ds((c + 1) * CB, CB)],
                                        direct01[rows, :].rearrange("p (b d) -> p b d", d=D),
                                        AX, ALU.add).then_inc(feat01_done, 1)

            def sum2(q):
                dve.wait_ge(direct2_out, q + 1)
                for i in range(2):
                    nc.vector.tensor_reduce(feat2[:, bass.ds(q * CB + i * (CB // 2), CB // 2)],
                                            direct2[H * i:H * (i + 1), :].rearrange("p (b d) -> p b d", d=D),
                                            AX, ALU.add).then_inc(feat2_done, 1)

            def w1_low_part():
                dve.wait_ge(w1_hi_made, 1)
                nc.vector.tensor_tensor(w1_lo[:].rearrange("p t o -> p (t o)"), w1_raw,
                                        w1_hi[:].rearrange("p t o -> p (t o)").bitcast(fp32),
                                        ALU.subtract).then_inc(w1_lo_made, 1)

            def turn(c, parity):
                layer0, layer1, layer2 = parts(c)

                def p0(k):
                    if layer0:
                        product0(c + 2, k)

                def p1(s):
                    if layer1:
                        product1(c + 1, 1 - parity, s)

                def p2(g):
                    if layer2:
                        product2(c, parity, g)

                if isinstance(c, int) and c == -1:
                    p1(0)
                    p1(1)
                    p1(2)
                    w1_low_part()
                    p0(0)
                    p1(3)
                    p1(4)
                    sum01(c, slice(0, H))
                    p1(5)
                    p0(1)
                    p0(2)
                    p1(6)
                    p0(3)
                    p1(7)
                    p1(8)
                    p1(9)
                    return
                p1(0)
                p1(1)
                p1(2)
                p0(0)
                p1(3)
                p1(4)
                if not isinstance(c, int) or 0 <= c < CHUNKS - 1:
                    sum01(c)
                elif c == CHUNKS - 1:
                    sum01(c, slice(H, 128))
                p0(1)
                p2(0)
                p0(2)
                p2(1)
                p1(5)
                p1(6)
                p1(7)
                if not isinstance(c, int) or c >= 1:
                    sum2(c - 1)
                p2(2)
                p0(3)
                p1(8)
                p1(9)
                p2(3)
                p2(4)

            nc.vector.memset(direct01[:, :], 0.0).then_inc(zeros_made, 1)
            nc.vector.memset(feat01[H:128, 0:CB], 0.0).then_inc(feat_cleared, 1)
            nc.vector.memset(feat01[0:H, B:B + CB], 0.0).then_inc(feat_cleared, 1)
            product0(0, 0)
            dve.wait_ge(w0_here, 32)
            nc.vector.tensor_tensor(w0_sb[:], w0a_raw.rearrange("p (t o) -> p t o", o=O),
                                    w0b_raw.rearrange("p (t o) -> p t o", o=O), ALU.add).then_inc(w0_summed, 1)
            for k in range(1, PAIRS):
                product0(0, k)
            turns(dve, turn, turn_from=-1)
            sum2(CHUNKS - 1)
            dve.wait_ge(y_done, 1)
            nc.vector.tensor_copy(y_sb, y_ps[0:1, :]).then_inc(y_copied, 1)

        @block.gpsimd
        def _(pool):
            def turn(c, parity):
                if not parts(c)[1]:
                    return
                for s in range(SPLITS):
                    if whole(c + 1, s):
                        continue
                    n, slot = split(c + 1, 1 - parity, s)
                    pool.wait_ge(z1_hi_made, splits(n))
                    if not isinstance(c, int) or n >= SPLIT_RING + WHOLE:
                        pool.wait_ge(z1_used, n - SPLIT_RING + 1)
                    nc.gpsimd.tensor_tensor(z1_lo[:, slot, :], z1[:, slot, :], z1_hi[:, slot, :].bitcast(fp32),
                                            ALU.subtract).then_inc(z1_lo_made, 1)

            turns(pool, turn)

        @block.scalar
        def _(act):
            def high_part(q, parity, s):
                n, slot = split(q, parity, s)
                act.wait_ge(z1_made, n + 1)
                if not isinstance(q, int) or n >= SPLIT_RING + WHOLE:
                    act.wait_ge(z1_used, n - SPLIT_RING + 1)
                nc.scalar.copy(z1_hi[:, slot, :], z1[:, slot, :]).then_inc(z1_hi_made, 1)

            def own_to_psum(q):
                act.wait_ge(own_here, 16 * (q + 1))
                if not isinstance(q, int) or q >= 1:
                    act.wait_ge(z0_made, PAIRS * q)
                nc.scalar.copy(own_ps[:, :], own[:, :]).then_inc(own_in_psum, 1)

            def evacuate(layer, acc, prev, direct_out, prev_made):
                nc.scalar.activation(direct01[H * layer:H * (layer + 1), :], acc[H:O, :], RELU,
                                     bias=bias_sb[H:O, layer:layer + 1]).then_inc(direct_out, 1)
                nc.scalar.activation(prev[0:H, :], acc[0:H, :], RELU, bias=bias_sb[0:H, layer:layer + 1])
                nc.scalar.activation(prev[H:O, :], acc[0:H, :], RELU,
                                     bias=bias_sb[0:H, layer:layer + 1]).then_inc(prev_made, 1)

            def evacuate0(q):
                act.wait_ge(z0_used, PAIRS * (q + 1))
                if not isinstance(q, int) or q >= 1:
                    act.wait_ge(feat01_done, q)
                    act.wait_ge(z1_made, SPLITS * q)
                evacuate(0, acc0, prev0, direct0_out, prev0_made)

            def evacuate1(q):
                act.wait_ge(z1_used, SPLITS * (q + 1))
                if not isinstance(q, int) or q >= 1:
                    act.wait_ge(z2_made, GROUPS * q)
                    act.wait_ge(feat01_done, q + 1)
                evacuate(1, acc1, prev1, direct1_out, prev1_made)

            def evacuate2(q):
                act.wait_ge(z2_used, GROUPS * (q + 1))
                if not isinstance(q, int) or q >= 1:
                    act.wait_ge(feat2_done, 2 * q)
                nc.scalar.activation(direct2[:, :], acc2[:, :], RELU, bias=bias_sb[:, 2:3]).then_inc(direct2_out, 1)

            def turn(c, parity):
                layer0, layer1, layer2 = parts(c)
                if isinstance(c, int) and c == -2:
                    own_to_psum(0)
                    act.wait_ge(small_here, 32)
                    evacuate0(0)
                    act.wait_ge(w1_here, 16)
                    nc.scalar.copy(w1_hi[:].rearrange("p t o -> p (t o)"), w1_raw).then_inc(w1_hi_made, 1)
                    return

                def high(s):
                    if layer1 and not whole(c + 1, s):
                        high_part(c + 1, 1 - parity, s)

                if isinstance(c, int) and c == -1:
                    own_to_psum(c + 2)
                    for s in range(WHOLE, SPLITS):
                        high(s)
                    evacuate0(c + 2)
                    return
                high(0)
                if layer0:
                    own_to_psum(c + 2)
                high(1)
                if layer2:
                    evacuate1(c)
                high(2)
                high(3)
                high(4)
                if not isinstance(c, int) or c >= 1:
                    evacuate2(c - 1)
                high(5)
                high(6)
                high(7)
                high(8)
                if layer0:
                    evacuate0(c + 2)
                high(9)

            turns(act, turn)
            evacuate2(CHUNKS - 1)

        @block.tensor
        def _(pe):
            def sums0(q, k):
                a, b = pair(k)
                if k == 0 and (not isinstance(q, int) or q >= 1):
                    pe.wait_ge(prev0_made, q)
                pe.wait_ge(z0_made, PAIRS * q + k + 1)
                for t in range(a, b):
                    last = nc.tensor.matmul(acc0[:, :], w0_sb[:, t, :],
                                            z0[:, k % RING, (t - a) * CHUNK:(t - a + 1) * CHUNK],
                                            start=t == 0, stop=t == T0 - 1)
                last.then_inc(z0_used, 1)

            def sums1(q, parity, s):
                n, slot = split(q, parity, s)
                if s == 0 and (not isinstance(q, int) or q >= 1):
                    pe.wait_ge(prev1_made, q)
                if whole(q, s):
                    pe.wait_ge(z1_made, n + 1)
                else:
                    pe.wait_ge(z1_lo_made, splits(n))
                for t in range(SPLIT):
                    at = slice(t * CHUNK, (t + 1) * CHUNK)
                    j = SPLIT * s + t
                    if whole(q, s):
                        last = nc.tensor.matmul(acc1[:, :], w1_raw[:, j * O:(j + 1) * O], z1[:, slot, at],
                                                start=j == 0, stop=False)
                        continue
                    nc.tensor.matmul(acc1[:, :], w1_hi[:, j, :], z1_hi[:, slot, at], start=j == 0, stop=False)
                    nc.tensor.matmul(acc1[:, :], w1_hi[:, j, :], z1_lo[:, slot, at], start=False, stop=False)
                    last = nc.tensor.matmul(acc1[:, :], w1_lo[:, j, :], z1_hi[:, slot, at],
                                            start=False, stop=j == T1 - 1)
                last.then_inc(z1_used, 1)

            def sums2(q, parity, g):
                slot = (GROUPS * parity + g) % RING
                if g == 0 and (not isinstance(q, int) or q >= 1):
                    pe.wait_ge(direct2_out, q)
                pe.wait_ge(z2_made, GROUPS * q + g + 1)
                for t in range(G):
                    j = G * g + t
                    for h in range(2):
                        at = t * CHUNK + h * HALF
                        last = nc.tensor.matmul(acc2[H * h:H * (h + 1), :], w2_sb[:, j, :],
                                                z2[:, slot, at:at + HALF], start=j == 0, stop=j == T1 - 1)
                last.then_inc(z2_used, 1)

            def turn(c, parity):
                layer0, layer1, layer2 = parts(c)
                if isinstance(c, int) and c == 0:
                    pe.wait_ge(w2_here, 16)

                def s0(k):
                    if layer0:
                        sums0(c + 2, k)

                def s1(s):
                    if layer1:
                        sums1(c + 1, 1 - parity, s)

                def s2(g):
                    if layer2:
                        sums2(c, parity, g)

                if isinstance(c, int) and c == -1:
                    pe.wait_ge(w1_here, 16)
                    s1(0)
                    s1(1)
                    s0(0)
                    s1(2)
                    s1(3)
                    s0(1)
                    pe.wait_ge(w1_lo_made, 1)
                    s1(4)
                    s1(5)
                    s0(2)
                    s1(6)
                    s0(3)
                    s1(7)
                    s1(8)
                    s1(9)
                    return
                s1(0)
                s0(0)
                s1(1)
                s0(1)
                s1(2)
                s2(0)
                s2(1)
                s1(3)
                s0(2)
                s1(4)
                s0(3)
                s2(2)
                s1(5)
                s1(6)
                s1(7)
                s1(8)
                s1(9)
                s2(3)
                s2(4)

            pe.wait_ge(zeros_made, 1)
            for _ in range(WARM_UPS):
                nc.tensor.matmul(acc0[:, :], direct01[:, 0:O], direct01[:, :], start=True, stop=True)
            pe.wait_ge(w0_summed, 1)
            turns(pe, turn)
            pe.wait_ge(small_here, 32)
            pe.wait_ge(feat_cleared, 2)
            pe.wait_ge(feat01_done, CHUNKS + 1)
            nc.tensor.matmul(y_ps[0:1, :], wl_sb[:, 0:1], feat01[:, 0:B], start=True, stop=False)
            nc.tensor.matmul(y_ps[0:1, :], wl_sb[:, 1:2], feat01[:, CB:B + CB], start=False, stop=False)
            pe.wait_ge(feat2_done, 2 * CHUNKS)
            nc.tensor.matmul(y_ps[0:1, :], wl_sb[0:H, 2:3], feat2[:, :], start=False, stop=True).then_inc(y_done, 1)


def kernel(r_x, L0_rec_w0, L0_rec_b0, L0_rec_w1, L0_rec_b1, L0_rec_w2, L0_rec_b2, L0_rec_wl):
    import numpy as np
    import concourse.bacc as bacc
    from concourse.bass_utils import run_bass_kernel_spmd

    fp32 = mybir.dt.float32
    xt = np.asarray(r_x).transpose(1, 0, 2).reshape(M, CHUNKS, CHUNK)
    start, tile = np.arange(STARTS)[:, None], np.arange(T0)[None, :]
    xs = xt[(start + SPT * tile) % M].transpose(2, 0, 1, 3)
    xf = xt.reshape(GROUPS, G, 2, CHUNKS, CHUNK).transpose(3, 0, 2, 1, 4)
    xf = np.repeat(xf[:, :, :, None], COPIES, 3)

    w0 = np.asarray(L0_rec_w0).reshape(O, M, M)
    m, i, t = np.meshgrid(np.arange(M), np.arange(SPT), np.arange(T0), indexing="ij")
    shift = SPT * t + i
    other = (m + shift) % M
    a = w0[:, m, other].transpose(1, 2, 3, 0)
    b = w0[:, other, m].transpose(1, 2, 3, 0)
    b = np.where(((shift == 0) | (shift == M // 2))[..., None], np.zeros_like(b), b)

    def rows12(w):
        return np.asarray(w).reshape(O, H, T1, 2).transpose(3, 1, 2, 0).reshape(128, T1, O)

    b0, b1, b2 = (np.asarray(v) for v in (L0_rec_b0, L0_rec_b1, L0_rec_b2))
    l0, l1, l2 = np.asarray(L0_rec_wl)[0].reshape(3, H)
    none = np.zeros_like(l0)
    arrays = {
        "xs": xs,
        "xf": xf,
        "w0a": a.reshape(P0, T0 * O),
        "w0b": b.reshape(P0, T0 * O),
        "w1": rows12(L0_rec_w1).reshape(128, T1 * O),
        "w2": rows12(L0_rec_w2)[:, :, H:],
        "bias": np.stack([b0, b1, np.concatenate([b2[H:], b2[H:]])], 1),
        "wl": np.stack([np.concatenate(v) for v in ([l0, none], [none, l1], [l2, none])], 1),
    }
    arrays = {k: np.ascontiguousarray(v) for k, v in arrays.items()}
    nc = bacc.Bacc("TRN2", target_bir_lowering=False, num_devices=1)
    args = [nc.dram_tensor(k, v.shape, fp32, kind="ExternalInput").ap() for k, v in arrays.items()]
    out = nc.dram_tensor("y", (B, 1), fp32, kind="ExternalOutput").ap()
    cin_kernel(nc, *args, out.rearrange("b one -> one b"))
    return run_bass_kernel_spmd(nc, [arrays], core_ids=[0]).results[0]["y"]
```
